# Optimizing a Trainium2 kernel written in Bass

```python
import numpy as np
import jax
import jax.numpy as jnp

def _softmax(x, axis=-1):
    return jax.nn.softmax(x, axis=axis)

def _gelu(x):
    return jax.nn.gelu(x, approximate=True)

def _silu(x):
    return jax.nn.silu(x)

def _sigmoid(x):
    return jax.nn.sigmoid(x)

def _layernorm(x, axis=-1, eps=1e-05):
    m = jnp.mean(x, axis=axis, keepdims=True)
    v = jnp.var(x, axis=axis, keepdims=True)
    return (x - m) / jnp.sqrt(v + eps)

def _scatter_add(tgt, idx, src, axis=0):
    return tgt.at[idx].add(src)

def _segment_sum(src, seg, n):
    return jax.ops.segment_sum(src, seg, n)
kernel_name = 'mk_prb_d1_jaxref_r4_186c12'

def setup_inputs(seed: int=0):
    np.random.seed(seed)
    _w = jnp.asarray

    def _L0_attn_setup():
        import jax, jax.numpy as jnp
        import numpy as np
        B, N, DIM, H = (2, 512, 256, 16)
        DH = DIM // H
        SCALE = DH ** (-0.5)

        def _rotary_emb(n, d, dtype):
            inv_freq = 1.0 / 10000.0 ** (jnp.arange(0, d, 2, dtype=jnp.float32) / d)
            freqs = jnp.outer(jnp.arange(n, dtype=jnp.float32), inv_freq)
            return jnp.concatenate([freqs, freqs], axis=-1).astype(dtype)

        def _rotate_half(x):
            x1, x2 = jnp.split(x, 2, axis=-1)
            return jnp.concatenate([-x2, x1], axis=-1)

        def _apply_rotary(freqs, t):
            return t * jnp.cos(freqs) + _rotate_half(t) * jnp.sin(freqs)
        key = jax.random.key(seed)
        ks = jax.random.split(key, 4)
        x = jax.random.normal(ks[0], (B, N, DIM), dtype=jnp.float32)
        Wq = jax.random.normal(ks[1], (DIM, DIM), dtype=jnp.float32) * DIM ** (-0.5)
        Wkv = jax.random.normal(ks[2], (DIM, DIM), dtype=jnp.float32) * DIM ** (-0.5)
        Wout = jax.random.normal(ks[3], (DIM, DIM), dtype=jnp.float32) * DIM ** (-0.5)
        bout = jnp.zeros((DIM,), dtype=jnp.float32)
        return {'x': x, 'Wq': Wq, 'Wkv': Wkv, 'Wout': Wout, 'bout': bout}
    _L0_attn_in = _L0_attn_setup()

    def _L0_ffn_setup():
        import jax, jax.numpy as jnp
        import numpy as np
        DIM = 256
        HIDDEN = 768
        SCALE = 1.0 / 127.0

        def _dequant(w_int, dtype):
            return w_int.astype(dtype) * jnp.asarray(SCALE, dtype)
        key = jax.random.key(seed)
        k_x, k_g, k_u, k_d = jax.random.split(key, 4)
        x = jax.random.normal(k_x, (4, 512, DIM), dtype=jnp.float32)
        w_gate = jax.random.randint(k_g, (HIDDEN, DIM), -127, 128, dtype=jnp.int32)
        w_up = jax.random.randint(k_u, (HIDDEN, DIM), -127, 128, dtype=jnp.int32)
        w_down = jax.random.randint(k_d, (DIM, HIDDEN), -127, 128, dtype=jnp.int32)
        return {'x': x, 'w_gate': w_gate, 'w_up': w_up, 'w_down': w_down}
    _L0_ffn_in = _L0_ffn_setup()
    _d = {'L0_attn_x': _L0_attn_in['x'], 'L0_attn_Wq': _L0_attn_in['Wq'], 'L0_attn_Wkv': _L0_attn_in['Wkv'], 'L0_attn_Wout': _L0_attn_in['Wout'], 'L0_attn_bout': _L0_attn_in['bout'], 'L0_ffn_w_gate': _L0_ffn_in['w_gate'], 'L0_ffn_w_up': _L0_ffn_in['w_up'], 'L0_ffn_w_down': _L0_ffn_in['w_down']}
    _x0 = _d['L0_attn_x']
    _d['L0_attn_x'] = jax.random.normal(jax.random.fold_in(jax.random.key(seed), 1), (4, 1024, 256), dtype=_x0.dtype)
    del _x0
    return _d

def reference(L0_attn_x, L0_attn_Wq, L0_attn_Wkv, L0_attn_Wout, L0_attn_bout, L0_ffn_w_gate, L0_ffn_w_up, L0_ffn_w_down):

    def _L0_attn_ref(x, Wq, Wkv, Wout, bout):
        import jax, jax.numpy as jnp
        import numpy as np
        B, N, DIM, H = (2, 512, 256, 16)
        DH = DIM // H
        SCALE = DH ** (-0.5)

        def _rotary_emb(n, d, dtype):
            inv_freq = 1.0 / 10000.0 ** (jnp.arange(0, d, 2, dtype=jnp.float32) / d)
            freqs = jnp.outer(jnp.arange(n, dtype=jnp.float32), inv_freq)
            return jnp.concatenate([freqs, freqs], axis=-1).astype(dtype)

        def _rotate_half(x):
            x1, x2 = jnp.split(x, 2, axis=-1)
            return jnp.concatenate([-x2, x1], axis=-1)

        def _apply_rotary(freqs, t):
            return t * jnp.cos(freqs) + _rotate_half(t) * jnp.sin(freqs)
        b, n, dim = x.shape
        q = x @ Wq
        kv = x @ Wkv
        split = lambda t: t.reshape(b, n, H, DH).transpose(0, 2, 1, 3).reshape(b * H, n, DH)
        q, kv = (split(q), split(kv))
        freqs = _rotary_emb(n, DH, x.dtype)[None]
        q = _apply_rotary(freqs, q)
        kv = _apply_rotary(freqs, kv)
        q = q * SCALE
        att = jnp.einsum('bmd,bnd->bmn', q, kv)
        attn = jax.nn.softmax(att, axis=-1)
        out = jnp.einsum('bij,bjd->bid', attn, kv)
        out = out.reshape(b, H, n, DH).transpose(0, 2, 1, 3).reshape(b, n, dim)
        return out @ Wout + bout

    def _L0_ffn_ref(x, w_gate, w_up, w_down):
        import jax, jax.numpy as jnp
        import numpy as np
        DIM = 256
        HIDDEN = 768
        SCALE = 1.0 / 127.0

        def _dequant(w_int, dtype):
            return w_int.astype(dtype) * jnp.asarray(SCALE, dtype)
        wg = _dequant(w_gate, x.dtype)
        wu = _dequant(w_up, x.dtype)
        wd = _dequant(w_down, x.dtype)
        gate = jnp.einsum('bsd,hd->bsh', x, wg)
        up = jnp.einsum('bsd,hd->bsh', x, wu)
        h = jax.nn.silu(gate) * up
        return jnp.einsum('bsh,dh->bsd', h, wd)
    x = L0_attn_x
    xn = _layernorm(x, axis=-1)
    x = x + _L0_attn_ref(xn, L0_attn_Wq, L0_attn_Wkv, L0_attn_Wout, L0_attn_bout) + _L0_ffn_ref(xn, L0_ffn_w_gate, L0_ffn_w_up, L0_ffn_w_down)
    return x

_drawn_inputs = setup_inputs


def setup_inputs(seed=0):
    import zlib

    import numpy as np

    out = dict(_drawn_inputs(seed))
    spreads = {'L0_attn_bout': (0.0, 0.8)}
    factors = {'L0_attn_Wq': 8.0, 'L0_attn_Wkv': 8.0, 'L0_attn_Wout': 8.0}
    for name, (base, spread) in spreads.items():
        noise = np.random.default_rng([zlib.crc32(name.encode()), seed]).standard_normal(out[name].shape)
        drawn = base * np.exp(spread * noise) if base else spread * noise
        out[name] = jnp.asarray(drawn.astype(out[name].dtype))
    for name, factor in factors.items():
        out[name] = (out[name] * factor).astype(out[name].dtype)
    return out
```

```python
from contextlib import ExitStack

import numpy as np

import concourse.bass as bass
from concourse import mybir

ALU = mybir.AluOpType
ACT = mybir.ActivationFunctionType
AX = mybir.AxisListType
F32 = mybir.dt.float32
BF16 = mybir.dt.bfloat16
FP16 = mybir.dt.float16
I32 = mybir.dt.int32

P = 128
BATCH, SEQ, DIM = 4, 1024, 256
HEADS, DH = 16, 16
HIDDEN = 768
EPS = 1e-5
DEQUANT = 1.0 / 127.0
H_SCALE = 0.25

CHUNK = 512
CT = CHUNK // P
CPB = SEQ // CHUNK
BT = SEQ // P
NCHUNK = BATCH * CPB
KD = DIM // P
KH = HIDDEN // P
HG = HEADS * DH // P
HPG = P // DH

PAIRS = BATCH * HEADS // 2
PPB = HEADS // 2
RING = 4
STEPS = BT
NPART = 3
PROD = 6 * DH
ROWS = PROD + NPART
MAXES = 2 * BT
LEAD = 12
T_AT = 5
QH = SEQ // CHUNK
PER_STEP = 2 * QH


def build(nc, x, w_q, w_kv, w_out, b_out, w_gate, w_up, w_down, rope, ident, out):
    xt = x.rearrange("b (t p) d -> b p t d", p=P)
    out_t = out.rearrange("b (t p) d -> b p t d", p=P)
    parts_d = nc.dram_tensor("parts_d", [2, NPART, BATCH, HG, P, SEQ], BF16).ap()
    parts_rows = parts_d.rearrange("o s b g (h d) n -> o s d (b g h) n", d=DH)
    v_d = nc.dram_tensor("v_d", [BATCH, P, BT, DIM], F32).ap()
    o_d = nc.dram_tensor("o_d", [PAIRS, PER_STEP, 2 * DH, CHUNK], F32).ap()
    o_rows = o_d.rearrange("p (a q) r n -> p a r q n", a=2)

    with ExitStack() as ctx:
        def sb(name, shape, dt):
            return ctx.enter_context(nc.sbuf_tensor(name, shape, dt))

        def sem(name):
            return ctx.enter_context(nc.semaphore(name))

        identf = sb("identf", [P, P], F32)
        identb = sb("identb", [P, P], BF16)
        rope_sb = sb("rope_sb", [P, BT, 2, 2, DH], F32)
        wqkv = sb("wqkv", [P, KD, 2 * DIM], F32)
        wo = sb("wo", [P, HG, DIM], F32)
        bias = sb("bias", [P, DIM], F32)
        wg = sb("wg", [P, KD, HIDDEN], FP16)
        wu = sb("wu", [P, KD, HIDDEN], FP16)
        wd = sb("wd", [P, KH, DIM], FP16)
        x_all = sb("x_all", [P, BATCH * BT, DIM], F32)
        v_all = sb("v_all", [P, BATCH * BT, DIM], F32)
        stats = sb("stats", [P, BATCH * BT, 6], F32)
        mv = sb("mv", [P, BATCH * BT, 2], F32)
        std = sb("std", [P, BATCH * BT], F32)
        rstd = sb("rstd", [P, BATCH * BT], F32)
        epsb = sb("epsb", [P, 1], F32)
        arena = sb("arena", [P, 15 * 1024], F32)
        zeros = sb("zeros", [P, MAXES], F32)

        used = [0]

        def carve(words, dt, pattern=None, **dims):
            a = arena[:, used[0]:used[0] + words]
            used[0] += words
            if dt != F32:
                a = a.bitcast(dt)
            return a.rearrange(pattern, **dims) if pattern else a

        int_g = carve(KD * HIDDEN, I32, "p (k n) -> p k n", k=KD)
        int_u = carve(KD * HIDDEN, I32, "p (k n) -> p k n", k=KD)
        int_d = carve(KH * DIM, I32, "p (k n) -> p k n", k=KH)
        xn = carve(CT * DIM, F32, "p (t d) -> p t d", t=CT)
        xnT = carve(KD * CHUNK, F32, "p (k n) -> p k n", k=KD)
        xh = carve(KD * CHUNK // 2, FP16, "p (k n) -> p k n", k=KD)
        xl = carve(KD * CHUNK // 2, FP16, "p (k n) -> p k n", k=KD)
        rope_a = [carve(2 * DIM, F32) for _ in range(2)]
        rope_b = [carve(2 * DIM, F32) for _ in range(2)]
        qk = carve(CT * 2 * DIM, F32, "p (t n) -> p t n", t=CT)
        used[0] = 0
        after_ints = 2 * KD * HIDDEN + KH * DIM
        rest = [carve(CHUNK, F32) for _ in range(4)]
        parts = [carve(NPART * CHUNK // 2, BF16, "p (s n) -> p s n", s=NPART) for _ in range(2)]
        assert used[0] <= after_ints
        used[0] = after_ints + 2 * CT * DIM + KD * CHUNK + 4 * 2 * DIM + CT * 2 * DIM
        parts += [carve(NPART * CHUNK // 2, BF16, "p (s n) -> p s n", s=NPART) for _ in range(2)]
        assert used[0] <= 15 * 1024
        gact = [sb(f"gact{i}", [P, CHUNK], F32) for i in range(2)]
        hid = [sb(f"hid{i}", [P, CHUNK], F32) for i in range(3)]
        hh = sb("hh", [P, KH, CHUNK], FP16)
        hl = sb("hl", [P, KH, CHUNK], FP16)
        qs = [sb(f"qs{i}", [ROWS, 2, SEQ], BF16) for i in range(RING)]
        ks = [sb(f"ks{i}", [ROWS, 2, SEQ], BF16) for i in range(RING)]
        negmax = [sb(f"negmax{i}", [P, MAXES], F32) for i in range(2)]
        mrest = sb("mrest", [P, 2, MAXES], F32)
        mparts = [sb(f"mparts{i}", [P, P], BF16) for i in range(2)]
        mrows = [sb(f"mrows{i}", [NPART * MAXES, P], BF16) for i in range(2)]
        used[0] = 0
        probs = [carve(CHUNK, F32) for _ in range(2 * PER_STEP)]
        vstage = [carve(2 * BT * 2 * DH, F32, "p (a k n) -> p a k n", a=2, k=BT) for _ in range(2)]
        osb = [carve(CHUNK, F32) for _ in range(2)]
        oall = [carve(HG * SEQ, F32, "p (g n) -> p g n", g=HG) for _ in range(2)]
        lall = [carve(HG * SEQ, F32, "p (g n) -> p g n", g=HG)]
        assert used[0] <= 15 * 1024
        res = [gact[0][:, 0:DIM], gact[1][:, 0:DIM], hid[0][:, 0:DIM], hid[1][:, 0:DIM]]

        ps = ctx.enter_context(nc.psum_tensor("ps", [P, 8, CHUNK], F32))

        consts_in = sem("consts_in")
        wqkv_in = sem("wqkv_in")
        ints_in = sem("ints_in")
        x_in = [sem(f"x_in{b}") for b in range(BATCH)]
        weights_ready = sem("weights_ready")
        stats_done = sem("stats_done")
        var_done = sem("var_done")
        std_done = sem("std_done")
        rstd_done = sem("rstd_done")
        xn_ready = sem("xn_ready")
        xT_ready = sem("xT_ready")
        xT_copied = sem("xT_copied")
        xl_ready = sem("xl_ready")
        biased = sem("biased")
        proj_done = sem("proj_done")
        rope_read = sem("rope_read")
        rope_done = sem("rope_done")
        v_stored = sem("v_stored")
        v_in = sem("v_in")
        gate_done = sem("gate_done")
        up_done = sem("up_done")
        silu_done = sem("silu_done")
        hid_done = sem("hid_done")
        hh_done = sem("hh_done")
        hl_done = sem("hl_done")
        turned = sem("turned")
        hi_done = sem("hi_done")
        rest_done = sem("rest_done")
        mid_done = sem("mid_done")
        lo_done = sem("lo_done")
        parts_stored = [sem(f"parts_stored{g}") for g in range(4)]
        down_done = sem("down_done")
        y_done = sem("y_done")

        ones_set = sem("ones_set")
        stacks_in = [sem(f"stacks_in{i}") for i in range(RING)]
        max_scores = sem("max_scores")
        max_done = sem("max_done")
        msplit = sem("msplit")
        msplit_done = sem("msplit_done")
        mturned = sem("mturned")
        mrows_done = sem("mrows_done")
        m_in = [sem(f"m_in{i}") for i in range(RING)]
        scores_done = sem("scores_done")
        exp_done = sem("exp_done")
        v_staged = sem("v_staged")
        pv_done = sem("pv_done")
        o_copied = sem("o_copied")
        o_stored = [sem(f"o_stored{i}") for i in range(2)]

        o_in = [sem(f"o_in{i}") for i in range(2)]
        l_in = sem("l_in")
        attn_ready = sem("attn_ready")
        wout_done = sem("wout_done")
        res_done = sem("res_done")
        res_stored = [sem(f"res_stored{i}") for i in range(4)]

        block = ctx.enter_context(nc.Block())

        def bank_proj(t):
            return ps[:, t, :]

        def bank_gate(j):
            return ps[:, (4 + 2 * j) % 8, :]

        def bank_up(j):
            return ps[:, (5 + 2 * j) % 8, :]

        def bank_x(k):
            return ps[:, k, :]

        def bank_turn(g):
            return ps[:, 2 + g, :]

        def bank_down(t):
            return ps[:, 6 + t // 2, (t % 2) * DIM:(t % 2 + 1) * DIM]

        def score_bank(s, j):
            return 4 + (4 * ((s - 1) % (RING * STEPS)) + j) % 3

        def bank_user_before(s, j):
            back = 1
            while True:
                n = 4 * s + j - back
                if n < 0:
                    return None
                if score_bank(n // 4, n % 4) == score_bank(s, j):
                    return back
                back += 1

        @block.sync
        def _(sp):
            def store_chunk(b, s):
                c = b * CPB + s
                for g in range(4):
                    sp.wait_ge(lo_done, 4 * c + g + 1)
                    dst = parts_d[g // HG, :, bass.ds(b, 1), g % HG, :, s * CHUNK:(s + 1) * CHUNK]
                    sp.dma_start(dst.rearrange("s o p n -> p (s o) n"), parts[g]).then_inc(parts_stored[g], 16)
                    if g == 0:
                        sp.dma_start(v_d[bass.ds(b, 1), :, s * CT:(s + 1) * CT, :].rearrange("o p t d -> p (o t) d"),
                                     qk[:, :, DIM:2 * DIM]).then_inc(v_stored, 16)

            def load_pair(p, ring):
                for dst, o, groups in ((qs, 0, ((0, 3, 0), (3, 2, 0), (5, 1, 0))),
                                       (ks, 1, ((0, 3, 0), (3, 2, 1), (5, 1, 2)))):
                    for row, n, part in groups:
                        for k in range(n):
                            which = part if o == 1 else k
                            sp.dma_start(dst[ring][(row + k) * DH:(row + k + 1) * DH, :, :],
                                         parts_rows[o, which, :, bass.ds(2 * p, 2), :]
                                         ).then_inc(stacks_in[ring], 16)

            def load_mrows(p, slot):
                sp.wait_ge(mrows_done, p + 1)
                sp.dma_start(qs[slot % RING][PROD:ROWS, :, :], mrows[slot % 2][:, :]
                             ).then_inc(m_in[slot % RING], 16)

            def store_o(p, slot):
                sp.wait_ge(o_copied, p + 1)
                sp.dma_start(o_d[bass.ds(p, 1), :, :, :].rearrange("o j r n -> (o j r) n"),
                             osb[slot % 2]).then_inc(o_stored[slot % 2], 16)

            for b in range(BATCH):
                sp.dma_start(x_all[:, b * BT:(b + 1) * BT, :], xt[b]).then_inc(x_in[b], 16)
                if b == 0:
                    sp.dma_start(identf[:, :], ident).then_inc(consts_in, 16)
                    sp.dma_start(wqkv[:, :, 0:DIM], w_q.rearrange("(k p) n -> p k n", p=P)).then_inc(wqkv_in, 16)
                    sp.dma_start(wqkv[:, :, DIM:], w_kv.rearrange("(k p) n -> p k n", p=P)).then_inc(wqkv_in, 16)
                    sp.dma_start(rope_sb[:, :, :, :, :], rope).then_inc(consts_in, 16)
                    sp.dma_start(bias[:, :], b_out.rearrange("(o n) -> o n", o=1).to_broadcast((P, DIM))
                                 ).then_inc(consts_in, 16)
                    sp.dma_start(int_g, w_gate.rearrange("(k p) n -> p k n", p=P)).then_inc(ints_in, 16)
                    sp.dma_start(int_u, w_up.rearrange("(k p) n -> p k n", p=P)).then_inc(ints_in, 16)
                    sp.dma_start(int_d, w_down.rearrange("(k p) n -> p k n", p=P)).then_inc(ints_in, 16)
            sp.dma_start(wo[:, :, :], w_out.rearrange("(g p) n -> p g n", p=P)).then_inc(consts_in, 16)
            with sp.Fori(0, BATCH - 1) as b:
                for s in range(CPB):
                    store_chunk(b, s)
            for g in range(4):
                sp.wait_ge(parts_stored[g], 16 * CPB)
            for p in range(RING - 1):
                load_pair(p, p)
            for s in range(CPB):
                store_chunk(BATCH - 1, s)
            sp.wait_ge(v_stored, 16 * NCHUNK)
            sp.wait_ge(y_done, CT * NCHUNK)
            for b in range(BATCH):
                sp.dma_start(v_all[:, b * BT:(b + 1) * BT, :], v_d[b]).then_inc(v_in, 16)
            for g in range(4):
                sp.wait_ge(parts_stored[g], 16 * NCHUNK)
            load_mrows(0, 0)

            def slot(p, j, load, rows):
                if load:
                    sp.wait_ge(scores_done, PER_STEP * STEPS * p)
                    load_pair(p + RING - 1, (j + RING - 1) % RING)
                if rows:
                    load_mrows(p + 1, j + 1)
                store_o(p, j)

            with sp.Fori(0, PAIRS // RING - 1) as i:
                for j in range(RING):
                    slot(i * RING + j, j, True, True)
            for j in range(RING):
                p = PAIRS - RING + j
                slot(p, j, p + RING - 1 < PAIRS, p + 1 < PAIRS)

            for i in range(2):
                sp.wait_ge(o_stored[i], 16 * PAIRS // 2)

            def load_sums(b, k):
                for dst, row, s in ((oall[k], 0, o_in[k]), (lall[0], DH, l_in)):
                    for g in range(HG):
                        for pp in range(PPB // HG):
                            for a in range(2):
                                at = pp * 2 * DH + a * DH
                                src = o_rows[bass.ds(b * PPB + g * (PPB // HG) + pp, 1), a, row:row + DH, :, :]
                                sp.dma_start(dst[at:at + DH, g, :].rearrange("d (q n) -> d q n", q=QH),
                                             src.rearrange("o d q n -> (o d) q n")).then_inc(s, 16)

            def store_res(b, k):
                for t in range(BT):
                    n = k * BT + t
                    sp.wait_ge(res_done, b * BT + t + 1)
                    sp.dma_start(out_t[bass.ds(b, 1), :, t, :].rearrange("o p d -> p (o d)"),
                                 res[n % 4]).then_inc(res_stored[n % 4], 16)

            for b in range(BATCH):
                if b >= 1:
                    sp.wait_ge(attn_ready, b)
                if b >= 2:
                    sp.wait_ge(wout_done, BT * (b - 1))
                load_sums(b, b % 2)
                if b >= 1:
                    store_res(b - 1, (b - 1) % 2)
            store_res(BATCH - 1, (BATCH - 1) % 2)
            for i in range(4):
                sp.wait_ge(res_stored[i], 16 * BATCH * BT // 4)

        @block.tensor
        def _(pe):
            def turn_x(c):
                pe.wait_ge(xn_ready, c + 1)
                for k in range(KD):
                    for t in range(CT):
                        mm = pe.transpose(bank_x(k)[:, t * P:(t + 1) * P], xn[:, t, k * P:(k + 1) * P], identf[:, :])
                    mm.then_inc(xT_ready, 1)

            def project(c):
                pe.wait_ge(xT_copied, 2 * KD * (c + 1))
                pe.wait_ge(rest_done, 4 * c)
                for t in range(CT):
                    for k in range(KD):
                        mm = pe.matmul(bank_proj(t), xnT[:, k, t * P:(t + 1) * P], wqkv[:, k, :],
                                       start=(k == 0), stop=(k == KD - 1))
                    mm.then_inc(proj_done, 1)

            def gate_up(c):
                pe.wait_ge(xl_ready, KD * (c + 1))
                for j in range(KH):
                    for which, w, bank, done in ((0, wg, bank_gate(j), gate_done), (1, wu, bank_up(j), up_done)):
                        if j == 1 and which == 0:
                            pe.wait_ge(y_done, CT * c)
                        if j == 2:
                            pe.wait_ge(rope_read, CT * c + 1 + which)
                        if j == 3:
                            pe.wait_ge(rope_read, CT * c + 3 + which)
                        if j >= 4:
                            pe.wait_ge((silu_done, hid_done)[which], KH * c + j - 3)
                        n = 0
                        for k in range(KD):
                            for xp in (xh, xl):
                                mm = pe.matmul(bank, w[:, k, j * P:(j + 1) * P], xp[:, k, :],
                                               start=(n == 0), stop=(n == 2 * KD - 1))
                                n += 1
                        mm.then_inc(done, 1)

            def turn_qk(c):
                for g in range(4):
                    if g == 0:
                        pe.wait_ge(rope_done, CT * (c + 1))
                    pe.wait_ge((silu_done, hid_done)[g % 2], KH * c + 4 + g // 2)
                    for t in range(CT):
                        mm = pe.transpose(bank_turn(g)[:, t * P:(t + 1) * P], qk[:, t, g * P:(g + 1) * P], identf[:, :])
                    mm.then_inc(turned, 1)

            def down(c):
                pe.wait_ge(hh_done, KH * (c + 1))
                pe.wait_ge(hl_done, KH * (c + 1))
                for t in range(CT):
                    for n in range(2 * KH):
                        hp = (hh, hl)[n // KH]
                        mm = pe.matmul(bank_down(t), hp[:, n % KH, t * P:(t + 1) * P], wd[:, n % KH, :],
                                       start=(n == 0), stop=(n == 2 * KH - 1))
                    mm.then_inc(down_done, 1)

            def chunk(c, last):
                project(c)
                gate_up(c)
                if not last:
                    pe.wait_ge(hid_done, KH * c + 3)
                    turn_x(c + 1)
                turn_qk(c)
                down(c)

            pe.wait_ge(consts_in, 64)
            turn_x(0)
            pe.wait_ge(wqkv_in, 32)
            pe.wait_ge(weights_ready, 4)
            with pe.Fori(0, BATCH - 1) as b:
                for s in range(CPB):
                    chunk(b * CPB + s, False)
            for s in range(CPB):
                chunk((BATCH - 1) * CPB + s, s == CPB - 1)

            def turn_max(p, slot_of):
                pe.wait_ge(msplit_done, p + 1)
                pe.transpose(ps[:, 0, 0:P // 2].bitcast(BF16), mparts[slot_of % 2][:, :], identb[:, :]
                             ).then_inc(mturned, 1)

            def scores(turn, ls, j):
                s = turn * RING * STEPS + ls
                ring = (ls // STEPS) % RING
                kt = ls % STEPS
                a, half = j // QH, j % QH
                back = bank_user_before(ls, j)
                if kt == 0 and j == 0:
                    pe.wait_ge(m_in[ring], 16 * (turn + ls // (RING * STEPS) + 1))
                if back is not None:
                    pe.wait_ge(exp_done, PER_STEP * s + j - back + 1)
                pe.matmul(ps[:, score_bank(ls, j), :], ks[ring][0:ROWS, a, kt * P:(kt + 1) * P],
                          qs[ring][0:ROWS, a, half * CHUNK:(half + 1) * CHUNK], start=True, stop=True
                          ).then_inc(scores_done, 1)

            def values(s, ls, p):
                kt = ls % STEPS
                if kt == 0:
                    pe.wait_ge(v_staged, p + 1)
                    pe.wait_ge(o_copied, p)
                pe.wait_ge(exp_done, PER_STEP * (s + 1))
                for j in range(PER_STEP):
                    mm = pe.matmul(ps[32 * j:32 * j + 32, 7, :], vstage[(ls // STEPS) % 2][:, j // QH, kt, :],
                                   probs[PER_STEP * (ls % 2) + j], start=(kt == 0), stop=(kt == STEPS - 1))
                mm.then_inc(pv_done, 1)

            def maxima(turn, m, h):
                pl, kt = m // STEPS, m % STEPS
                p, ring, k = turn * RING + pl, pl % RING, 2 * kt + h
                n = MAXES * p + k
                a, i = k // BT, k % BT
                if k == 0:
                    pe.wait_ge(stacks_in[ring], 16 * 12 * (turn + pl // RING + 1))
                if not isinstance(n, int) or n >= 2:
                    pe.wait_ge(max_done, n - 1)
                for half in range(QH):
                    mm = pe.matmul(ps[:, 2 * (k % 2) + half, :], qs[ring][0:PROD, a, i * P:(i + 1) * P],
                                   ks[ring][0:PROD, a, half * CHUNK:(half + 1) * CHUNK], start=True, stop=True)
                mm.then_inc(max_scores, 1)

            def step(turn, ls, last_turn=False):
                s = turn * RING * STEPS + ls
                p = turn * RING + ls // STEPS
                m = ls + LEAD
                more = not last_turn or m < RING * STEPS
                if ls % STEPS == T_AT and more_pairs(ls, last_turn):
                    even = min(2 * m - 1, MAXES * RING) if last_turn else 2 * m - 1
                    pe.wait_ge(max_done, MAXES * turn * RING + even)
                    turn_max(p + 1, ls // STEPS + 1)
                scores(turn, ls, 0)
                scores(turn, ls, 1)
                if more:
                    if ls % STEPS == T_AT and more_pairs(ls, last_turn):
                        pe.wait_ge(mrows_done, p + 2)
                    maxima(turn, m, 0)
                scores(turn, ls, 2)
                scores(turn, ls, 3)
                if more:
                    maxima(turn, m, 1)
                if not (isinstance(s, int) and s == 0):
                    values(s - 1, ls - 1, turn * RING + (ls - 1) // STEPS)

            def more_pairs(ls, last_turn):
                return not last_turn or ls // STEPS + 1 < RING

            pe.wait_ge(ones_set, RING)
            pe.wait_ge(y_done, CT * NCHUNK)
            pe.wait_ge(rest_done, 4 * NCHUNK)
            for m in range(LEAD):
                if m == LEAD - 3:
                    pe.wait_ge(max_done, 2 * m - 1)
                    turn_max(0, 0)
                    pe.wait_ge(mrows_done, 1)
                for h in range(2):
                    maxima(0, m, h)
            step(0, 0)
            with pe.Fori(0, PAIRS // RING - 1) as i:
                for ls in range(1, RING * STEPS + 1):
                    step(i, ls)
            for ls in range(1, RING * STEPS):
                step(PAIRS // RING - 1, ls, True)
            values(PAIRS * STEPS - 1, RING * STEPS - 1, PAIRS - 1)

            for b in range(BATCH):
                pe.wait_ge(attn_ready, b + 1)
                if b == 0:
                    pe.wait_ge(exp_done, PER_STEP * PAIRS * STEPS)
                    pe.wait_ge(o_copied, PAIRS)
                for t in range(BT):
                    n = b * BT + t
                    if n >= 8:
                        pe.wait_ge(res_done, n - 7)
                    for g in range(HG):
                        mm = pe.matmul(ps[:, n % 8, 0:DIM], oall[b % 2][:, g, t * P:(t + 1) * P], wo[:, g, :],
                                       start=(g == 0), stop=(g == HG - 1))
                    mm.then_inc(wout_done, 1)

        @block.scalar
        def _(act):
            def copy_x(c):
                for k in range(KD):
                    act.wait_ge(xT_ready, KD * c + k + 1)
                    act.activation(xnT[:, k, :], bank_x(k), ACT.Copy).then_inc(xT_copied, 1)
                    act.activation(xh[:, k, :], bank_x(k), ACT.Copy).then_inc(xT_copied, 1)

            def silu(c, j):
                act.wait_ge(gate_done, KH * c + j + 1)
                act.wait_ge(hid_done, KH * c + max(j - 1, 0))
                act.activation(gact[j % 2][:, :], bank_gate(j), ACT.Silu, scale=DEQUANT).then_inc(silu_done, 1)

            def high(c, j):
                if j == 0:
                    act.wait_ge(down_done, CT * c)
                act.wait_ge(hid_done, KH * c + j + 1)
                act.activation(hh[:, j, :], hid[j % 3][:, :], ACT.Copy).then_inc(hh_done, 1)

            def chunk(c, last):
                for j in range(KH):
                    silu(c, j)
                    if j >= 1:
                        high(c, j - 1)
                high(c, KH - 1)
                if not last:
                    copy_x(c + 1)
                for g in range(4):
                    act.wait_ge(turned, 4 * c + g + 1)
                    act.wait_ge(parts_stored[g], 16 * c)
                    act.activation(parts[g][:, 0, :], bank_turn(g), ACT.Copy).then_inc(hi_done, 1)
                for g in range(4):
                    act.wait_ge(rest_done, 4 * c + g + 1)
                    act.activation(parts[g][:, 1, :], rest[g], ACT.Copy).then_inc(mid_done, 1)

            act.wait_ge(var_done, BATCH * BT + 1)
            act.activation(std[:, :], mv[:, :, 1], ACT.Sqrt, bias=epsb[:, 0:1]).then_inc(std_done, 1)
            act.wait_ge(weights_ready, 4)
            copy_x(0)
            with act.Fori(0, BATCH - 1) as b:
                for s in range(CPB):
                    chunk(b * CPB + s, False)
            for s in range(CPB):
                chunk((BATCH - 1) * CPB + s, s == CPB - 1)

            def exps(turn, ls):
                s = turn * RING * STEPS + ls
                if not (isinstance(s, int) and s <= 1):
                    act.wait_ge(pv_done, s - 1)
                for j in range(PER_STEP):
                    act.wait_ge(scores_done, PER_STEP * s + j + 1)
                    act.activation(probs[PER_STEP * (ls % 2) + j], ps[:, score_bank(ls, j), :], ACT.Exp
                                   ).then_inc(exp_done, 1)

            def copy_o(p, slot, turn):
                act.wait_ge(pv_done, STEPS * (p + 1))
                if not (isinstance(p, int) and p < 2):
                    act.wait_ge(o_stored[slot % 2], 16 * (turn * (RING // 2) + slot // 2))
                act.activation(osb[slot % 2], ps[:, 7, :], ACT.Copy).then_inc(o_copied, 1)

            act.wait_ge(y_done, CT * NCHUNK)
            for g in range(4):
                act.wait_ge(parts_stored[g], 16 * NCHUNK)
            exps(0, 0)
            with act.Fori(0, PAIRS // RING - 1) as i:
                for ls in range(1, RING * STEPS + 1):
                    exps(i, ls)
                    if ls % STEPS == 0:
                        copy_o(i * RING + ls // STEPS - 1, ls // STEPS - 1, i)
            t = PAIRS // RING - 1
            for ls in range(1, RING * STEPS):
                exps(t, ls)
                if ls % STEPS == 0:
                    copy_o(t * RING + ls // STEPS - 1, ls // STEPS - 1, t)
            copy_o(PAIRS - 1, RING - 1, t)

        @block.vector
        def _(dve):
            dve.memset(epsb[:, :], EPS).then_inc(var_done, 1)
            for b in range(BATCH):
                dve.wait_ge(x_in[b], 16)
                for t in range(BT):
                    n = b * BT + t
                    dve.bn_stats(stats[:, n, :], x_all[:, n, :]).then_inc(stats_done, 1)
                    if t >= 1:
                        dve.wait_ge(stats_done, n)
                        dve.bn_aggr(mv[:, n - 1, :], stats[:, n - 1, :]).then_inc(var_done, 1)
                dve.wait_ge(stats_done, n + 1)
                dve.bn_aggr(mv[:, n, :], stats[:, n, :]).then_inc(var_done, 1)
            dve.wait_ge(std_done, 1)
            dve.reciprocal(rstd[:, :], std[:, :]).then_inc(rstd_done, 1)
            dve.wait_ge(rstd_done, 1)
            dve.wait_ge(consts_in, 64)

            def normalise(turn, first):
                for t in range(CT):
                    n = turn * BT + first * CT + t
                    ins = dve.tensor_scalar(xn[:, t, :], x_all[:, bass.ds(n, 1), :].rearrange("p o d -> p (o d)"),
                                            mv[:, bass.ds(n, 1), 0:1].rearrange("p o d -> p (o d)"),
                                            rstd[:, bass.ds(n, 1)],
                                            ALU.subtract, ALU.mult)
                ins.then_inc(xn_ready, 1)
                dve.wait_ge(xn_ready, turn * CPB + first + 1)
                for t in range(CT):
                    n = turn * BT + first * CT + t
                    row = x_all[:, bass.ds(n, 1), :].rearrange("p o d -> p (o d)")
                    dve.tensor_tensor(row, row, bias[:, :], ALU.add).then_inc(biased, 1)

            def rotate(c, s, t):
                dve.wait_ge(proj_done, CT * c + t + 1)
                src = bank_proj(t).rearrange("p (o h d) -> p o h d", o=2, d=DH)
                a = rope_a[t % 2].rearrange("p (o h d) -> p o h d", o=2, d=DH)
                b = rope_b[t % 2].rearrange("p (o h d) -> p o h d", o=2, d=DH)
                cos = rope_sb[:, s * CT + t, 0, :, :].unsqueeze(2).to_broadcast((P, 2, HEADS, DH))
                sin = rope_sb[:, s * CT + t, 1, :, :].unsqueeze(2).to_broadcast((P, 2, HEADS, DH))
                half = DH // 2
                dve.wait_ge(rope_done, CT * c + max(t - 1, 0))
                dve.tensor_tensor(a, src, cos, ALU.mult)
                dve.tensor_tensor(b[:, :, :, 0:half], src[:, :, :, half:DH], sin[:, :, :, 0:half], ALU.mult)
                dve.tensor_tensor(b[:, :, :, half:DH], src[:, :, :, 0:half], sin[:, :, :, half:DH], ALU.mult
                                  ).then_inc(rope_read, 1)

            def rotated(c, t):
                if t == 0:
                    dve.wait_ge(turned, 4 * c)
                    dve.wait_ge(v_stored, 16 * c)
                dve.wait_ge(rope_read, CT * c + t + 1)
                dve.tensor_tensor(qk[:, t, :], rope_a[t % 2], rope_b[t % 2], ALU.add).then_inc(rope_done, 1)

            def low_x(c):
                for k in range(KD):
                    dve.wait_ge(xT_copied, 2 * KD * c + 2 * k + 2)
                    dve.tensor_tensor(xl[:, k, :], xnT[:, k, :], xh[:, k, :], ALU.subtract).then_inc(xl_ready, 1)

            def chunk(turn, s, last):
                c = turn * CPB + s
                for t in range(CT):
                    rotate(c, s, t)
                    if t >= 1:
                        rotated(c, t - 1)
                rotated(c, CT - 1)
                if not last:
                    dve.wait_ge(xT_ready, KD * (c + 1))
                    normalise(turn, s + 1)
                for j in range(KH):
                    dve.wait_ge(silu_done, KH * c + j + 1)
                    dve.wait_ge(up_done, KH * c + j + 1)
                    dve.wait_ge(hh_done, KH * c + max(j - 2, 0))
                    dve.wait_ge(hl_done, KH * c + max(j - 2, 0))
                    dve.scalar_tensor_tensor(hid[j % 3][:, :], bank_up(j), DEQUANT * H_SCALE, gact[j % 2][:, :],
                                             ALU.mult, ALU.mult).then_inc(hid_done, 1)
                if not last:
                    low_x(c + 1)
                for g in range(4):
                    dve.wait_ge(hi_done, 4 * c + g + 1)
                    dve.wait_ge(mid_done, 4 * c)
                    dve.wait_ge(lo_done, 4 * c)
                    dve.tensor_tensor(rest[g], bank_turn(g), parts[g][:, 0, :], ALU.subtract).then_inc(rest_done, 1)
                for t in range(CT):
                    dve.wait_ge(down_done, CT * c + t // 2 * 2 + 2)
                    if t == 0:
                        dve.wait_ge(biased, CT * (c + 1))
                    row = x_all[:, bass.ds(turn * BT + s * CT + t, 1), :].rearrange("p o d -> p (o d)")
                    dve.scalar_tensor_tensor(row, bank_down(t), DEQUANT / H_SCALE, row, ALU.mult, ALU.add
                                             ).then_inc(y_done, 1)

            dve.tensor_copy(identb[:, :], identf[:, :]).then_inc(weights_ready, 1)
            normalise(0, 0)
            dve.wait_ge(ints_in, 48)
            for w, i in ((wg, int_g), (wu, int_u), (wd, int_d)):
                dve.tensor_copy(w[:, :, :], i).then_inc(weights_ready, 1)
            low_x(0)
            with dve.Fori(0, BATCH - 1) as b:
                for s in range(CPB):
                    chunk(b, s, False)
            for s in range(CPB):
                chunk(BATCH - 1, s, s == CPB - 1)

            def maxima(turn, m, h):
                pl, k = m // STEPS, 2 * (m % STEPS) + h
                p = turn * RING + pl
                n = MAXES * p + k
                dve.wait_ge(max_scores, n + 1)
                if k == 0 and not (isinstance(p, int) and p < 2):
                    dve.wait_ge(msplit_done, p - 1)
                dve.tensor_reduce(negmax[pl % 2][:, k:k + 1], ps[:, 2 * (k % 2):2 * (k % 2) + 2, :],
                                  AX.XY, ALU.max, negate=True).then_inc(max_done, 1)

            def rows(p, slot, turn):
                dve.wait_ge(mturned, p + 1)
                if not (isinstance(p, int) and p < 2):
                    dve.wait_ge(m_in[(slot - 2) % RING], 16 * (turn + (slot - 2) // RING + 1))
                n = NPART * MAXES
                dve.tensor_copy(mrows[slot % 2][:, :], ps[0:n, 0, 0:P // 2].bitcast(BF16)).then_inc(mrows_done, 1)

            def step(turn, ls, last_turn=False):
                m = ls + LEAD
                if ls % STEPS == T_AT and (not last_turn or ls // STEPS + 1 < RING):
                    rows(turn * RING + ls // STEPS + 1, ls // STEPS + 1, turn)
                if not last_turn or m < RING * STEPS:
                    maxima(turn, m, 0)
                    maxima(turn, m, 1)

            for m in range(LEAD):
                if m == LEAD - 3:
                    rows(0, 0, 0)
                maxima(0, m, 0)
                maxima(0, m, 1)
            step(0, 0)
            with dve.Fori(0, PAIRS // RING - 1) as i:
                for ls in range(1, RING * STEPS + 1):
                    step(i, ls)
            for ls in range(1, RING * STEPS):
                step(PAIRS // RING - 1, ls, True)

            def normalise_sums(b):
                dve.wait_ge(l_in, 16 * 16 * (b + 1))
                dve.reciprocal(lall[0], lall[0]).then_inc(rstd_done, 1)
                dve.wait_ge(o_in[b % 2], 16 * 16 * (b // 2 + 1))
                dve.wait_ge(rstd_done, b + 2)
                dve.tensor_tensor(oall[b % 2], oall[b % 2], lall[0], ALU.mult).then_inc(attn_ready, 1)

            for b in range(BATCH):
                normalise_sums(b)
                for t in range(BT):
                    n = b * BT + t
                    dve.wait_ge(wout_done, n + 1)
                    if n >= 4:
                        dve.wait_ge(res_stored[n % 4], 16 * (n // 4))
                    dve.tensor_tensor(res[n % 4], ps[:, n % 8, 0:DIM], x_all[:, n, :], ALU.add).then_inc(res_done, 1)

        @block.gpsimd
        def _(pool):
            pool.memset(zeros[:, :], 0.0).then_inc(msplit, 1)
            for i in range(2):
                pool.wait_ge(msplit, i + 1)
                pool.memset(mparts[i][:, :], 0.0).then_inc(msplit, 1)
            pool.wait_ge(msplit, 3)
            for i in range(RING):
                pool.memset(ks[i][PROD:ROWS, :, :], 1.0).then_inc(ones_set, 1)
                pool.wait_ge(ones_set, i + 1)

            def chunk(c):
                for j in range(KH):
                    pool.wait_ge(hh_done, KH * c + j + 1)
                    pool.tensor_tensor(hl[:, j, :], hid[j % 3][:, :], hh[:, j, :], ALU.subtract).then_inc(hl_done, 1)
                for g in range(4):
                    pool.wait_ge(mid_done, 4 * c + g + 1)
                    pool.tensor_tensor(parts[g][:, 2, :], rest[g], parts[g][:, 1, :], ALU.subtract
                                       ).then_inc(lo_done, 1)

            with pool.Fori(0, BATCH) as b:
                for s in range(CPB):
                    chunk(b * CPB + s)

            def stage_values(p, batch, slot, pair):
                for a in range(2):
                    src = v_all[:, bass.ds(batch * BT, BT), bass.ds(pair * 2 * DH + a * DH, DH)]
                    ins = pool.tensor_copy(vstage[slot % 2][:, a, :, 0:DH], src)
                ins.then_inc(v_staged, 1)

            def split_max(p, slot):
                pool.wait_ge(max_done, MAXES * (p + 1))
                if not (isinstance(p, int) and p < 2):
                    pool.wait_ge(mturned, p - 1)
                nm, mp = negmax[slot % 2][:, :], mparts[slot % 2]
                mc = [mp[:, k * MAXES:(k + 1) * MAXES] for k in range(NPART)]
                n = 4 * p + 3
                pool.tensor_tensor(mc[0], nm, zeros[:, :], ALU.add).then_inc(msplit, 1)
                pool.wait_ge(msplit, n + 1)
                pool.tensor_tensor(mrest[:, 0, :], nm, mc[0], ALU.subtract).then_inc(msplit, 1)
                pool.wait_ge(msplit, n + 2)
                pool.tensor_tensor(mc[1], mrest[:, 0, :], zeros[:, :], ALU.add).then_inc(msplit, 1)
                pool.wait_ge(msplit, n + 3)
                pool.tensor_tensor(mc[2], mrest[:, 0, :], mc[1], ALU.subtract).then_inc(msplit, 1)
                pool.wait_ge(msplit, n + 4)
                pool.tensor_tensor(mrest[:, 1, :], zeros[:, :], zeros[:, :], ALU.add).then_inc(msplit_done, 1)

            pool.wait_ge(y_done, CT * NCHUNK)
            for g in range(4):
                pool.wait_ge(parts_stored[g], 16 * NCHUNK)
            for i in range(2):
                pool.memset(vstage[i][:, :, :, DH:2 * DH], 1.0).then_inc(ones_set, 1)
                pool.wait_ge(ones_set, RING + i + 1)
            split_max(0, 0)
            pool.wait_ge(v_in, 16 * BATCH)
            stage_values(0, 0, 0, 0)

            def slot(turn, j):
                p = turn * RING + j + 1
                split_max(p, j + 1)
                pool.wait_ge(pv_done, STEPS * (p - 1))
                q = j + 1
                stage_values(p, p_batch(turn, q), q, p_pair(turn, q))

            def p_batch(turn, q):
                return (turn * RING + q) // PPB

            def p_pair(turn, q):
                return (turn * RING + q) % PPB

            with pool.Fori(0, PAIRS // RING - 1) as i:
                for j in range(RING):
                    slot(i, j)
            for j in range(RING - 1):
                slot(PAIRS // RING - 1, j)


def rotary_tables():
    inv = np.float32(1.0) / np.power(10000.0, np.arange(0, DH, 2) / DH).astype(np.float32)
    angle = np.outer(np.arange(SEQ, dtype=np.float32), inv).astype(np.float32)
    angle = np.concatenate([angle, angle], axis=-1)
    sign = np.where(np.arange(DH) < DH // 2, -1.0, 1.0).astype(np.float32)
    cos, sin = np.cos(angle), np.sin(angle) * sign
    scale = np.array([DH ** -0.5, 1.0], np.float32)
    both = np.stack([cos, sin], 1)[:, :, None, :] * scale[None, None, :, None]
    both = both.reshape(BT, P, 2, 2, DH).transpose(1, 0, 2, 3, 4)
    return np.ascontiguousarray(both.astype(np.float32))


def kernel(L0_attn_x, L0_attn_Wq, L0_attn_Wkv, L0_attn_Wout, L0_attn_bout,
           L0_ffn_w_gate, L0_ffn_w_up, L0_ffn_w_down):
    import concourse.bacc as bacc
    from concourse.bass_utils import run_bass_kernel_spmd

    laid_out = {
        "x": np.asarray(L0_attn_x),
        "w_q": np.asarray(L0_attn_Wq),
        "w_kv": np.asarray(L0_attn_Wkv),
        "w_out": np.asarray(L0_attn_Wout),
        "b_out": np.asarray(L0_attn_bout),
        "w_gate": np.asarray(L0_ffn_w_gate).T,
        "w_up": np.asarray(L0_ffn_w_up).T,
        "w_down": np.asarray(L0_ffn_w_down).T,
        "rope": rotary_tables(),
        "ident": np.eye(P, dtype=np.float32),
    }
    nc = bacc.Bacc("TRN2", target_bir_lowering=False, num_devices=1)
    arrays, args = {}, []
    for name, a in laid_out.items():
        a = np.ascontiguousarray(a)
        arrays[f"{name}_dram"] = a
        args.append(nc.dram_tensor(f"{name}_dram", a.shape, mybir.dt.from_np(a.dtype), kind="ExternalInput").ap())
    args.append(nc.dram_tensor("out_dram", (BATCH, SEQ, DIM), F32, kind="ExternalOutput").ap())
    build(nc, *args)
    r = run_bass_kernel_spmd(nc, [arrays], core_ids=[0])
    return r.results[0]["out_dram"]
```

```python
from contextlib import ExitStack

import numpy as np

import concourse.bass as bass
from concourse import mybir

ALU = mybir.AluOpType
ACT = mybir.ActivationFunctionType
AX = mybir.AxisListType
F32 = mybir.dt.float32
BF16 = mybir.dt.bfloat16
FP16 = mybir.dt.float16
I32 = mybir.dt.int32

P = 128
BATCH, SEQ, DIM = 4, 1024, 256
HEADS, DH = 16, 16
HIDDEN = 768
EPS = 1e-5
DEQUANT = 1.0 / 127.0
H_SCALE = 0.25

CHUNK = 512
CT = CHUNK // P
CPB = SEQ // CHUNK
BT = SEQ // P
NCHUNK = BATCH * CPB
KD = DIM // P
KH = HIDDEN // P
HG = HEADS * DH // P
HPG = P // DH

PAIRS = BATCH * HEADS // 2
PPB = HEADS // 2
RING = 4
STEPS = BT
NPART = 3
PROD = 6 * DH
ROWS = PROD + NPART
MAXES = 2 * BT
LEAD = 11
T_AT = 6
INV_AT = 3
TILE_AT = 3
FIRST_SLOT = 2
FIRST = FIRST_SLOT * STEPS + 1
TURNS = PAIRS // RING - 1
LAG = 10
TILES_FROM = (LAG - FIRST_SLOT) // RING
LAST = FIRST_SLOT + TURNS * RING
CREDIT = 2
QH = SEQ // CHUNK
PER_STEP = 2 * QH


def build(nc, x, w_q, w_kv, w_out, b_out, w_gate, w_up, w_down, rope, ident, out):
    xt = x.rearrange("b (t p) d -> b p t d", p=P)
    out_t = out.rearrange("b (t p) d -> b p t d", p=P)
    parts_d = nc.dram_tensor("parts_d", [2, BATCH * HEADS, NPART * DH, SEQ], BF16).ap()
    parts_rows = parts_d.rearrange("o h r n -> o r h n")
    v_d = nc.dram_tensor("v_d", [BATCH, P, BT, DIM], F32).ap()
    o_d = nc.dram_tensor("o_d", [BATCH, HG, P, SEQ], F32).ap()
    o_heads = o_d.rearrange("b g (h d) (q n) -> (b g h) d q n", d=DH, q=QH)
    inv_d = nc.dram_tensor("inv_d", [BATCH * HEADS, SEQ], F32).ap()
    inv_groups = inv_d.rearrange("(b g h) n -> b g h n", g=HG, h=HPG)

    with ExitStack() as ctx:
        def sb(name, shape, dt):
            return ctx.enter_context(nc.sbuf_tensor(name, shape, dt))

        def sem(name):
            return ctx.enter_context(nc.semaphore(name))

        identf = sb("identf", [P, P], F32)
        identb = sb("identb", [P, P], BF16)
        rope_sb = sb("rope_sb", [P, BT, 2, 2, DH], F32)
        wqkv = sb("wqkv", [P, KD, 2 * DIM], F32)
        wo = sb("wo", [P, HG, DIM], F32)
        bias = sb("bias", [P, DIM], F32)
        wg = sb("wg", [P, KD, HIDDEN], FP16)
        wu = sb("wu", [P, KD, HIDDEN], FP16)
        wd = sb("wd", [P, KH, DIM], FP16)
        x_all = sb("x_all", [P, BATCH * BT, DIM], F32)
        v_all = sb("v_all", [P, BATCH * BT, DIM], F32)
        stats = sb("stats", [P, BATCH * BT, 6], F32)
        mv = sb("mv", [P, BATCH * BT, 2], F32)
        std = sb("std", [P, BATCH * BT], F32)
        rstd = sb("rstd", [P, BATCH * BT], F32)
        epsb = sb("epsb", [P, 1], F32)
        arena = sb("arena", [P, 15 * 1024], F32)
        zeros = sb("zeros", [P, MAXES], F32)

        used = [0]

        def carve(words, dt, pattern=None, **dims):
            a = arena[:, used[0]:used[0] + words]
            used[0] += words
            if dt != F32:
                a = a.bitcast(dt)
            return a.rearrange(pattern, **dims) if pattern else a

        int_g = carve(KD * HIDDEN, I32, "p (k n) -> p k n", k=KD)
        int_u = carve(KD * HIDDEN, I32, "p (k n) -> p k n", k=KD)
        int_d = carve(KH * DIM, I32, "p (k n) -> p k n", k=KH)
        xn = carve(CT * DIM, F32, "p (t d) -> p t d", t=CT)
        xnT = carve(KD * CHUNK, F32, "p (k n) -> p k n", k=KD)
        xh = carve(KD * CHUNK // 2, FP16, "p (k n) -> p k n", k=KD)
        xl = carve(KD * CHUNK // 2, FP16, "p (k n) -> p k n", k=KD)
        rope_a = [carve(2 * DIM, F32) for _ in range(2)]
        rope_b = [carve(2 * DIM, F32) for _ in range(2)]
        qk = carve(CT * 2 * DIM, F32, "p (t n) -> p t n", t=CT)
        used[0] = 0
        after_ints = 2 * KD * HIDDEN + KH * DIM
        rest = [carve(CHUNK, F32) for _ in range(4)]
        parts = [carve(NPART * CHUNK // 2, BF16, "p (s n) -> p s n", s=NPART) for _ in range(2)]
        assert used[0] <= after_ints
        used[0] = after_ints + 2 * CT * DIM + KD * CHUNK + 4 * 2 * DIM + CT * 2 * DIM
        parts += [carve(NPART * CHUNK // 2, BF16, "p (s n) -> p s n", s=NPART) for _ in range(2)]
        assert used[0] <= 15 * 1024
        gact = [sb(f"gact{i}", [P, CHUNK], F32) for i in range(2)]
        hid = [sb(f"hid{i}", [P, CHUNK], F32) for i in range(3)]
        hh = sb("hh", [P, KH, CHUNK], FP16)
        hl = sb("hl", [P, KH, CHUNK], FP16)
        qs = [sb(f"qs{i}", [ROWS, 2, SEQ], BF16) for i in range(RING)]
        ks = [sb(f"ks{i}", [ROWS, 2, SEQ], BF16) for i in range(RING)]
        negmax = [sb(f"negmax{i}", [P, MAXES], F32) for i in range(2)]
        mrest = sb("mrest", [P, 2, MAXES], F32)
        mparts = [sb(f"mparts{i}", [P, P], BF16) for i in range(2)]
        mrows = [sb(f"mrows{i}", [NPART * MAXES, P], BF16) for i in range(2)]
        used[0] = 0
        probs = [carve(CHUNK, F32) for _ in range(2 * PER_STEP)]
        vstage = [carve(2 * BT * 2 * DH, F32, "p (a k n) -> p a k n", a=2, k=BT) for _ in range(2)]
        osb = [carve(CHUNK, F32) for _ in range(2)]
        sums = [carve(SEQ * 2 // P, F32) for _ in range(2)]
        invs = [carve(SEQ * 2 // P, F32) for _ in range(2)]
        otile = [carve(HG * P, F32, "p (g n) -> p g n", g=HG) for _ in range(2)]
        itile = [carve(HG * P, F32, "p (g n) -> p g n", g=HG) for _ in range(2)]
        atile = [carve(HG * P, F32, "p (g n) -> p g n", g=HG) for _ in range(2)]
        res = [carve(DIM, F32) for _ in range(2)]
        assert used[0] <= 15 * 1024
        used[0] = 0
        olast = [carve(HG * CHUNK, F32, "p (g n) -> p g n", g=HG) for _ in range(2)]
        ilast = [carve(HG * CHUNK, F32, "p (g n) -> p g n", g=HG) for _ in range(2)]
        rlast = carve(BT * DIM, F32, "p (t d) -> p t d", t=BT)
        assert used[0] <= 15 * 1024

        ps = ctx.enter_context(nc.psum_tensor("ps", [P, 8, CHUNK], F32))

        consts_in = sem("consts_in")
        wqkv_in = sem("wqkv_in")
        ints_in = sem("ints_in")
        x_in = [sem(f"x_in{c}") for c in range(NCHUNK)]
        weights_ready = sem("weights_ready")
        stats_done = sem("stats_done")
        var_done = sem("var_done")
        std_done = sem("std_done")
        rstd_done = sem("rstd_done")
        xn_ready = sem("xn_ready")
        xT_ready = sem("xT_ready")
        xT_copied = sem("xT_copied")
        xl_ready = sem("xl_ready")
        biased = sem("biased")
        proj_done = sem("proj_done")
        rope_read = sem("rope_read")
        rope_done = sem("rope_done")
        v_stored = sem("v_stored")
        v_in = sem("v_in")
        gate_done = sem("gate_done")
        up_done = sem("up_done")
        silu_done = sem("silu_done")
        hid_done = sem("hid_done")
        hh_done = sem("hh_done")
        hl_done = sem("hl_done")
        turned = sem("turned")
        hi_done = sem("hi_done")
        rest_done = sem("rest_done")
        mid_done = sem("mid_done")
        lo_done = sem("lo_done")
        parts_stored = [sem(f"parts_stored{g}") for g in range(4)]
        down_done = sem("down_done")
        y_done = sem("y_done")

        ones_set = sem("ones_set")
        stacks_in = [sem(f"stacks_in{i}") for i in range(RING)]
        max_scores = sem("max_scores")
        max_done = sem("max_done")
        msplit = sem("msplit")
        msplit_done = sem("msplit_done")
        mturned = sem("mturned")
        mrows_done = sem("mrows_done")
        m_in = [sem(f"m_in{i}") for i in range(RING)]
        scores_done = sem("scores_done")
        exp_done = sem("exp_done")
        v_staged = sem("v_staged")
        pv_done = sem("pv_done")
        o_copied = sem("o_copied")
        o_stored = [sem(f"o_stored{i}") for i in range(2)]

        inv_done = sem("inv_done")
        inv_stored = [sem(f"inv_stored{i}") for i in range(2)]
        tile_in = [sem(f"tile_in{i}") for i in range(2)]
        divided = sem("divided")
        wout_done = sem("wout_done")
        res_done = sem("res_done")
        res_free = [sem(f"res_free{i}") for i in range(2)]
        last_in = [sem(f"last_in{i}") for i in range(2)]
        last_divided = sem("last_divided")
        last_res = sem("last_res")
        last_stored = sem("last_stored")

        block = ctx.enter_context(nc.Block())

        def bank_proj(t):
            return ps[:, t, :]

        def bank_gate(j):
            return ps[:, (4 + 2 * j) % 8, :]

        def bank_up(j):
            return ps[:, (5 + 2 * j) % 8, :]

        def bank_x(k):
            return ps[:, k, :]

        def bank_turn(g):
            return ps[:, 2 + g, :]

        def bank_down(t):
            return ps[:, 6 + t // 2, (t % 2) * DIM:(t % 2 + 1) * DIM]

        def score_bank(s, j):
            return 4 + (4 * ((s - FIRST) % (RING * STEPS)) + j) % 3

        def bank_user_before(s, j):
            back = 1
            while True:
                n = 4 * s + j - back
                if n < 0:
                    return None
                if score_bank(n // 4, n % 4) == score_bank(s, j):
                    return back
                back += 1

        def late_tile(ls):
            at = (TILE_AT, TILE_AT + 2)
            if ls % STEPS not in at:
                return None
            n = LAST - LAG + 2 * (ls // STEPS - FIRST_SLOT) + at.index(ls % STEPS)
            return n, n % 2

        @block.sync
        def _(sp):
            def store_chunk(b, s):
                c = b * CPB + s
                for g in range(4):
                    sp.wait_ge(lo_done, 4 * c + g + 1)
                    for k in range(NPART):
                        dst = parts_d[g // HG, bass.ds((b * HG + g % HG) * HPG, HPG), k * DH:(k + 1) * DH,
                                      s * CHUNK:(s + 1) * CHUNK]
                        sp.dma_start(dst, parts[g][:, k, :]).then_inc(parts_stored[g], 16)
                    if g == 0:
                        sp.dma_start(v_d[bass.ds(b, 1), :, s * CT:(s + 1) * CT, :].rearrange("o p t d -> p (o t) d"),
                                     qk[:, :, DIM:2 * DIM]).then_inc(v_stored, 16)

            def load_pair(p, ring):
                for row, n, part in ((0, 3, 0), (3, 2, 1), (5, 1, 2)):
                    at = slice(row * DH, (row + n) * DH)
                    sp.dma_start(qs[ring][at, :, :], parts_rows[0, 0:n * DH, bass.ds(2 * p, 2), :]
                                 ).then_inc(stacks_in[ring], 16)
                    for a in range(2):
                        src = parts_rows[1, part * DH:(part + 1) * DH, bass.ds(2 * p + a, 1), :]
                        sp.dma_start(ks[ring][at, a, :], src.rearrange("d o n -> o d n").to_broadcast((n, DH, SEQ))
                                     ).then_inc(stacks_in[ring], 16)

            def load_mrows(p, slot):
                sp.wait_ge(mrows_done, p + 1)
                sp.dma_start(qs[slot % RING][PROD:ROWS, :, :], mrows[slot % 2][:, :]
                             ).then_inc(m_in[slot % RING], 16)

            def store_o(p, slot):
                sp.wait_ge(o_copied, p + 1)
                sp.dma_start(sums[slot % 2], osb[slot % 2][DH:DH + 32 * (PER_STEP - 1) + 1:32, :]
                             ).then_inc(o_stored[slot % 2], 16)
                for q in range(PER_STEP):
                    sp.dma_start(o_heads[bass.ds(2 * p + q // QH, 1), :, q % QH, :].rearrange("o d n -> (o d) n"),
                                 osb[slot % 2][32 * q:32 * q + DH, :]).then_inc(o_stored[slot % 2], 16)

            def store_inv(p, slot):
                sp.wait_ge(inv_done, p + 1)
                sp.dma_start(inv_d[bass.ds(2 * p, 2), :], invs[slot % 2]).then_inc(inv_stored[slot % 2], 16)

            def load_tile(b, t, k):
                tok = bass.ds(t * P, P)
                sp.dma_start(otile[k], o_d[bass.ds(b, 1), :, :, tok].rearrange("o g p n -> p (o g) n")
                             ).then_inc(tile_in[k], 16)
                for g in range(HG):
                    src = inv_groups[bass.ds(b, 1), g, :, tok].rearrange("o h n -> (o h) n")
                    sp.dma_start(itile[k][:, g, :], src.unsqueeze(1).to_broadcast((HPG, DH, P))
                                 ).then_inc(tile_in[k], 16)

            def store_res(b, t, n, k):
                sp.wait_ge(res_done, n + 1)
                sp.dma_start(out_t[bass.ds(b, 1), :, bass.ds(t, 1), :].rearrange("o p t d -> p (o t d)"),
                             res[k]).then_inc(res_free[k], 16)

            for c in range(NCHUNK):
                sp.dma_start(x_all[:, c * CT:(c + 1) * CT, :],
                             xt[c // CPB][:, c % CPB * CT:(c % CPB + 1) * CT, :]).then_inc(x_in[c], 16)
                if c == 1:
                    sp.dma_start(identf[:, :], ident).then_inc(consts_in, 16)
                    sp.dma_start(bias[:, :], b_out.rearrange("(o n) -> o n", o=1).to_broadcast((P, DIM))
                                 ).then_inc(consts_in, 16)
                    sp.dma_start(wqkv[:, :, 0:DIM], w_q.rearrange("(k p) n -> p k n", p=P)).then_inc(wqkv_in, 16)
                    sp.dma_start(wqkv[:, :, DIM:], w_kv.rearrange("(k p) n -> p k n", p=P)).then_inc(wqkv_in, 16)
                    sp.dma_start(rope_sb[:, :, :, :, :], rope).then_inc(consts_in, 16)
                    sp.dma_start(int_g, w_gate.rearrange("(k p) n -> p k n", p=P)).then_inc(ints_in, 16)
                    sp.dma_start(int_u, w_up.rearrange("(k p) n -> p k n", p=P)).then_inc(ints_in, 16)
                    sp.dma_start(int_d, w_down.rearrange("(k p) n -> p k n", p=P)).then_inc(ints_in, 16)
            for g in range(HG):
                sp.dma_start(wo[:, g, :], w_out[g * P:(g + 1) * P, :]).then_inc(res_free[g], 16)
            store_chunk(0, 0)
            with sp.Fori(0, BATCH - 1) as i:
                store_chunk(i, 1)
                store_chunk(i + 1, 0)
            for g in range(4):
                sp.wait_ge(parts_stored[g], 16 * NPART * CPB)
            for p in range(2):
                load_pair(p, p)
            store_chunk(BATCH - 1, 1)
            sp.wait_ge(v_stored, 16 * NCHUNK)
            sp.wait_ge(y_done, CT * NCHUNK)
            for b in range(BATCH):
                sp.dma_start(v_all[:, b * BT:(b + 1) * BT, :], v_d[b]).then_inc(v_in, 16)
            for g in range(4):
                sp.wait_ge(parts_stored[g], 16 * NPART * NCHUNK)
            load_mrows(0, 0)

            def slot(p, j, load, rows, tiles):
                for b, t, n, k in tiles:
                    sp.wait_ge(divided, CREDIT + n - 1)
                    if n is tiles[0][2]:
                        m = (j + 1) % 2
                        sp.wait_ge(inv_stored[m], 16 * ((p - 3 - m) // 2 + 1))
                    load_tile(b, t, k)
                if not isinstance(p, int) or p >= 1:
                    store_o(p - 1, j - 1)
                if load:
                    if not isinstance(p, int) or p >= 2:
                        sp.wait_ge(scores_done, PER_STEP * STEPS * (p - 1))
                    load_pair(p + 2, (j + 2) % RING)
                if not isinstance(p, int) or p >= 1:
                    store_inv(p - 1, j - 1)
                for b, t, n, k in tiles:
                    store_res(b, t, n, k)
                if rows:
                    load_mrows(p + 1, j + 1)

            for p in range(FIRST_SLOT):
                slot(p, p, True, True, [])
            with sp.Fori(0, TILES_FROM) as i:
                for j in range(FIRST_SLOT, FIRST_SLOT + RING):
                    slot(i * RING + j, j, True, True, [])
            with sp.Fori(0, TURNS - TILES_FROM) as i:
                for j in range(RING):
                    tile = (i // 2, i % 2 * RING + j, i * RING + j, j % 2)
                    slot(i * RING + LAG + j, LAG + j, True, True, [tile])
            for j in range(LAST, PAIRS):
                n = LAST - LAG + 2 * (j - LAST)
                slot(j, j, False, j + 1 < PAIRS, [(m // BT, m % BT, m, m % 2) for m in (n, n + 1)])

            store_o(PAIRS - 1, PAIRS - 1)
            store_inv(PAIRS - 1, PAIRS - 1)
            for k in range(2):
                sp.wait_ge(inv_stored[k], 16 * PAIRS // 2)
            for k in range(CPB):
                tok = slice(k * CHUNK, (k + 1) * CHUNK)
                sp.dma_start(olast[k], o_d[BATCH - 1, :, :, tok].rearrange("g p n -> p g n")).then_inc(last_in[k], 16)
                for g in range(HG):
                    src = inv_groups[BATCH - 1, g, :, tok]
                    sp.dma_start(ilast[k][:, g, :], src.unsqueeze(1).to_broadcast((HPG, DH, CHUNK))
                                 ).then_inc(last_in[k], 16)
            for k in range(4):
                two = slice(2 * k, 2 * k + 2)
                sp.wait_ge(last_res, 2 * k + 2)
                sp.dma_start(out_t[BATCH - 1][:, two, :], rlast[:, two, :]).then_inc(last_stored, 16)
            sp.wait_ge(last_stored, 16 * 4)
            for k in range(2):
                sp.wait_ge(res_free[k], 16 * (1 + (BATCH - 1) * BT // 2))

        @block.tensor
        def _(pe):
            def turn_x(c):
                pe.wait_ge(xn_ready, c + 1)
                for k in range(KD):
                    for t in range(CT):
                        mm = pe.transpose(bank_x(k)[:, t * P:(t + 1) * P], xn[:, t, k * P:(k + 1) * P], identf[:, :])
                        if isinstance(c, int) and c + k + t == 0:
                            mm.then_inc(wout_done, CREDIT)
                    mm.then_inc(xT_ready, 1)

            def project(c):
                pe.wait_ge(xT_copied, 2 * KD * (c + 1))
                pe.wait_ge(rest_done, 4 * c)
                for t in range(CT):
                    for k in range(KD):
                        mm = pe.matmul(bank_proj(t), xnT[:, k, t * P:(t + 1) * P], wqkv[:, k, :],
                                       start=(k == 0), stop=(k == KD - 1))
                    mm.then_inc(proj_done, 1)

            def gate_up(c):
                pe.wait_ge(xl_ready, KD * (c + 1))
                for j in range(KH):
                    for which, w, bank, done in ((0, wg, bank_gate(j), gate_done), (1, wu, bank_up(j), up_done)):
                        if j == 1 and which == 0:
                            pe.wait_ge(y_done, CT * c)
                        if j == 2:
                            pe.wait_ge(rope_read, CT * c + 1 + which)
                        if j == 3:
                            pe.wait_ge(rope_read, CT * c + 3 + which)
                        if j >= 4:
                            pe.wait_ge((silu_done, hid_done)[which], KH * c + j - 3)
                        n = 0
                        for k in range(KD):
                            for xp in (xh, xl):
                                mm = pe.matmul(bank, w[:, k, j * P:(j + 1) * P], xp[:, k, :],
                                               start=(n == 0), stop=(n == 2 * KD - 1))
                                n += 1
                        mm.then_inc(done, 1)

            def turn_qk(c):
                for g in range(4):
                    if g == 0:
                        pe.wait_ge(rope_done, CT * (c + 1))
                    pe.wait_ge((silu_done, hid_done)[g % 2], KH * c + 4 + g // 2)
                    for t in range(CT):
                        mm = pe.transpose(bank_turn(g)[:, t * P:(t + 1) * P], qk[:, t, g * P:(g + 1) * P], identf[:, :])
                    mm.then_inc(turned, 1)

            def down(c):
                pe.wait_ge(hh_done, KH * (c + 1))
                pe.wait_ge(hl_done, KH * (c + 1))
                for t in range(CT):
                    for n in range(2 * KH):
                        hp = (hh, hl)[n // KH]
                        mm = pe.matmul(bank_down(t), hp[:, n % KH, t * P:(t + 1) * P], wd[:, n % KH, :],
                                       start=(n == 0), stop=(n == 2 * KH - 1))
                    mm.then_inc(down_done, 1)

            def chunk(c, last):
                project(c)
                gate_up(c)
                if not last:
                    pe.wait_ge(hid_done, KH * c + 3)
                    turn_x(c + 1)
                turn_qk(c)
                down(c)

            pe.wait_ge(consts_in, 48)
            turn_x(0)
            pe.wait_ge(wqkv_in, 32)
            pe.wait_ge(weights_ready, 4)
            chunk(0, False)
            with pe.Fori(0, BATCH - 1) as i:
                for s in (1, 2):
                    chunk(i * CPB + s, False)
            chunk(NCHUNK - 1, True)

            def turn_max(p, slot_of):
                pe.wait_ge(msplit_done, p + 1)
                pe.transpose(ps[:, 0, 0:P // 2].bitcast(BF16), mparts[slot_of % 2][:, :], identb[:, :]
                             ).then_inc(mturned, 1)

            def scores(turn, ls, j):
                s = turn * RING * STEPS + ls
                ring = (ls // STEPS) % RING
                kt = ls % STEPS
                a, half = j // QH, j % QH
                back = bank_user_before(ls, j)
                if kt == 0 and j == 0:
                    pe.wait_ge(m_in[ring], 16 * (turn + ls // (RING * STEPS) + 1))
                if back is not None:
                    pe.wait_ge(exp_done, PER_STEP * s + j - back + 1)
                pe.matmul(ps[:, score_bank(ls, j), :], ks[ring][0:ROWS, a, kt * P:(kt + 1) * P],
                          qs[ring][0:ROWS, a, half * CHUNK:(half + 1) * CHUNK], start=True, stop=True
                          ).then_inc(scores_done, 1)

            def values(s, ls, p):
                kt = ls % STEPS
                if kt == 0:
                    pe.wait_ge(v_staged, p + 1)
                    pe.wait_ge(o_copied, p)
                pe.wait_ge(exp_done, PER_STEP * (s + 1))
                for j in range(PER_STEP):
                    mm = pe.matmul(ps[32 * j:32 * j + 32, 7, :], vstage[(ls // STEPS) % 2][:, j // QH, kt, :],
                                   probs[PER_STEP * (ls % 2) + j], start=(kt == 0), stop=(kt == STEPS - 1))
                mm.then_inc(pv_done, 1)

            def maxima(turn, m, h):
                pl, kt = m // STEPS, m % STEPS
                p, ring, k = turn * RING + pl, pl % RING, 2 * kt + h
                n = MAXES * p + k
                a, i = k // BT, k % BT
                if k == 0:
                    pe.wait_ge(stacks_in[ring], 16 * 3 * NPART * (turn + pl // RING + 1))
                if not isinstance(n, int) or n >= 2:
                    pe.wait_ge(max_done, n - 1)
                for half in range(QH):
                    mm = pe.matmul(ps[:, 2 * (k % 2) + half, :], qs[ring][0:PROD, a, i * P:(i + 1) * P],
                                   ks[ring][0:PROD, a, half * CHUNK:(half + 1) * CHUNK], start=True, stop=True)
                mm.then_inc(max_scores, 1)

            def project_tile(n, k):
                pe.wait_ge(divided, CREDIT + n + 1)
                for g in range(HG):
                    mm = pe.matmul(ps[:, 0, 0:DIM], atile[k][:, g, :], wo[:, g, :], start=(g == 0), stop=(g == HG - 1))
                mm.then_inc(wout_done, 1)

            def step(turn, ls, last_turn=False, tile=None):
                s = turn * RING * STEPS + ls
                p = turn * RING + ls // STEPS
                m = ls + LEAD
                more = not last_turn or m < RING * STEPS
                if ls % STEPS == T_AT and more_pairs(ls, last_turn):
                    even = min(2 * m - 1, MAXES * RING) if last_turn else 2 * m - 1
                    pe.wait_ge(max_done, MAXES * turn * RING + even)
                    if last_turn and m >= RING * STEPS:
                        pe.wait_ge(res_done, late_tile(ls - 1)[0] + 1)
                    turn_max(p + 1, ls // STEPS + 1)
                if tile:
                    even = min(2 * m - 1, MAXES * RING) if last_turn else 2 * m - 1
                    pe.wait_ge(max_done, MAXES * turn * RING + even)
                    if last_turn:
                        pe.wait_ge(res_done, tile[0])
                        pe.wait_ge(mrows_done, PAIRS if ls >= (RING - 1) * STEPS else min(p + 1 + (ls % STEPS > T_AT), PAIRS))
                    project_tile(*tile)
                scores(turn, ls, 0)
                scores(turn, ls, 1)
                if more:
                    if ls % STEPS == T_AT and more_pairs(ls, last_turn):
                        pe.wait_ge(mrows_done, p + 2)
                    if tile:
                        pe.wait_ge(res_done, tile[0] + 1)
                    maxima(turn, m, 0)
                scores(turn, ls, 2)
                scores(turn, ls, 3)
                if more:
                    maxima(turn, m, 1)
                if not (isinstance(s, int) and s == 0):
                    values(s - 1, ls - 1, turn * RING + (ls - 1) // STEPS)

            def more_pairs(ls, last_turn):
                return not last_turn or ls // STEPS + 1 < RING

            pe.wait_ge(ones_set, RING)
            pe.wait_ge(y_done, CT * NCHUNK)
            pe.wait_ge(rest_done, 4 * NCHUNK)
            for m in range(LEAD):
                if m == T_AT + LEAD - STEPS:
                    pe.wait_ge(max_done, 2 * m - 1)
                    turn_max(0, 0)
                    pe.wait_ge(mrows_done, 1)
                for h in range(2):
                    maxima(0, m, h)
            for ls in range(FIRST):
                step(0, ls)
            with pe.Fori(0, TILES_FROM) as i:
                for ls in range(FIRST, FIRST + RING * STEPS):
                    step(i, ls)
            with pe.Fori(0, TURNS - TILES_FROM) as i:
                for ls in range(FIRST, FIRST + RING * STEPS):
                    j = ls // STEPS - FIRST_SLOT
                    step(i + TILES_FROM, ls, tile=(i * RING + j, j % 2) if ls % STEPS == TILE_AT else None)
            for ls in range(FIRST, RING * STEPS):
                step(TURNS, ls, True, late_tile(ls))
            values(PAIRS * STEPS - 1, RING * STEPS - 1, PAIRS - 1)

            pe.wait_ge(exp_done, PER_STEP * PAIRS * STEPS)
            pe.wait_ge(o_copied, PAIRS)
            pe.wait_ge(res_done, (BATCH - 1) * BT)
            for t in range(BT):
                pe.wait_ge(last_divided, t // CT + 1)
                for g in range(HG):
                    mm = pe.matmul(ps[:, t, 0:DIM], olast[t // CT][:, g, t % CT * P:(t % CT + 1) * P], wo[:, g, :],
                                   start=(g == 0), stop=(g == HG - 1))
                mm.then_inc(wout_done, 1)

        @block.scalar
        def _(act):
            def copy_x(c):
                for k in range(KD):
                    act.wait_ge(xT_ready, KD * c + k + 1)
                    act.activation(xnT[:, k, :], bank_x(k), ACT.Copy).then_inc(xT_copied, 1)
                    act.activation(xh[:, k, :], bank_x(k), ACT.Copy).then_inc(xT_copied, 1)

            def silu(c, j):
                act.wait_ge(gate_done, KH * c + j + 1)
                act.wait_ge(hid_done, KH * c + max(j - 1, 0))
                act.activation(gact[j % 2][:, :], bank_gate(j), ACT.Silu, scale=DEQUANT).then_inc(silu_done, 1)

            def high(c, j):
                if j == 0:
                    act.wait_ge(down_done, CT * c)
                act.wait_ge(hid_done, KH * c + j + 1)
                act.activation(hh[:, j, :], hid[j % 3][:, :], ACT.Copy).then_inc(hh_done, 1)

            def chunk(c, last):
                for j in range(KH):
                    silu(c, j)
                    if j >= 1:
                        high(c, j - 1)
                high(c, KH - 1)
                if isinstance(c, int) and c == 0:
                    roots(BT, BATCH * BT)
                if not last:
                    copy_x(c + 1)
                for g in range(4):
                    act.wait_ge(turned, 4 * c + g + 1)
                    act.wait_ge(parts_stored[g], 16 * NPART * c)
                    act.activation(parts[g][:, 0, :], bank_turn(g), ACT.Copy).then_inc(hi_done, 1)
                for g in range(4):
                    act.wait_ge(rest_done, 4 * c + g + 1)
                    act.activation(parts[g][:, 1, :], rest[g], ACT.Copy).then_inc(mid_done, 1)

            def roots(a, b):
                act.wait_ge(var_done, b + 1)
                act.activation(std[:, a:b], mv[:, a:b, 1], ACT.Sqrt, bias=epsb[:, 0:1]).then_inc(std_done, 1)

            roots(0, BT)
            act.wait_ge(weights_ready, 4)
            copy_x(0)
            chunk(0, False)
            with act.Fori(0, BATCH - 1) as i:
                for s in (1, 2):
                    chunk(i * CPB + s, False)
            chunk(NCHUNK - 1, True)

            def exps(turn, ls):
                s = turn * RING * STEPS + ls
                if not (isinstance(s, int) and s <= 1):
                    act.wait_ge(pv_done, s - 1)
                for j in range(PER_STEP):
                    act.wait_ge(scores_done, PER_STEP * s + j + 1)
                    act.activation(probs[PER_STEP * (ls % 2) + j], ps[:, score_bank(ls, j), :], ACT.Exp
                                   ).then_inc(exp_done, 1)

            def copy_o(p, slot, turn):
                act.wait_ge(pv_done, STEPS * (p + 1))
                if not (isinstance(p, int) and p < 2):
                    act.wait_ge(o_stored[slot % 2], 16 * (PER_STEP + 1) * (turn * (RING // 2) + slot // 2))
                act.activation(osb[slot % 2], ps[:, 7, :], ACT.Copy).then_inc(o_copied, 1)

            act.wait_ge(y_done, CT * NCHUNK)
            for g in range(4):
                act.wait_ge(parts_stored[g], 16 * NPART * NCHUNK)
            def steps(turn, first, end):
                for ls in range(first, end):
                    exps(turn, ls)
                    if ls % STEPS == 0 and ls:
                        q = ls // STEPS - 1
                        copy_o(turn * RING + q, q, turn)

            steps(0, 0, FIRST)
            with act.Fori(0, TURNS) as i:
                steps(i, FIRST, FIRST + RING * STEPS)
            steps(TURNS, FIRST, RING * STEPS)
            copy_o(PAIRS - 1, RING - 1, TURNS)

        @block.vector
        def _(dve):
            dve.memset(epsb[:, :], EPS).then_inc(var_done, 1)

            def moments(first, n):
                for t in range(first, first + n):
                    if t % CT == 0:
                        dve.wait_ge(x_in[t // CT], 16)
                    dve.bn_stats(stats[:, t, :], x_all[:, t, :]).then_inc(stats_done, 1)
                    if t > first:
                        dve.wait_ge(stats_done, t)
                        dve.bn_aggr(mv[:, t - 1, :], stats[:, t - 1, :]).then_inc(var_done, 1)
                dve.wait_ge(stats_done, t + 1)
                dve.bn_aggr(mv[:, t, :], stats[:, t, :]).then_inc(var_done, 1)

            def inverse(k, a, b):
                dve.wait_ge(std_done, k + 1)
                dve.reciprocal(rstd[:, a:b], std[:, a:b]).then_inc(rstd_done, 1)
                dve.wait_ge(rstd_done, k + 1)

            moments(0, BT)
            inverse(0, 0, BT)
            dve.wait_ge(consts_in, 48)

            def normalise(turn, first):
                for t in range(CT):
                    n = turn * BT + first * CT + t
                    ins = dve.tensor_scalar(xn[:, t, :], x_all[:, bass.ds(n, 1), :].rearrange("p o d -> p (o d)"),
                                            mv[:, bass.ds(n, 1), 0:1].rearrange("p o d -> p (o d)"),
                                            rstd[:, bass.ds(n, 1)],
                                            ALU.subtract, ALU.mult)
                ins.then_inc(xn_ready, 1)
                dve.wait_ge(xn_ready, turn * CPB + first + 1)
                for t in range(CT):
                    n = turn * BT + first * CT + t
                    row = x_all[:, bass.ds(n, 1), :].rearrange("p o d -> p (o d)")
                    dve.tensor_tensor(row, row, bias[:, :], ALU.add).then_inc(biased, 1)

            def rotate(c, s, t):
                dve.wait_ge(proj_done, CT * c + t + 1)
                src = bank_proj(t).rearrange("p (o h d) -> p o h d", o=2, d=DH)
                a = rope_a[t % 2].rearrange("p (o h d) -> p o h d", o=2, d=DH)
                b = rope_b[t % 2].rearrange("p (o h d) -> p o h d", o=2, d=DH)
                cos = rope_sb[:, s % CPB * CT + t, 0, :, :].unsqueeze(2).to_broadcast((P, 2, HEADS, DH))
                sin = rope_sb[:, s % CPB * CT + t, 1, :, :].unsqueeze(2).to_broadcast((P, 2, HEADS, DH))
                half = DH // 2
                dve.wait_ge(rope_done, CT * c + max(t - 1, 0))
                dve.tensor_tensor(a, src, cos, ALU.mult)
                dve.tensor_tensor(b[:, :, :, 0:half], src[:, :, :, half:DH], sin[:, :, :, 0:half], ALU.mult)
                dve.tensor_tensor(b[:, :, :, half:DH], src[:, :, :, 0:half], sin[:, :, :, half:DH], ALU.mult
                                  ).then_inc(rope_read, 1)

            def rotated(c, t):
                if t == 0:
                    dve.wait_ge(turned, 4 * c)
                    dve.wait_ge(v_stored, 16 * c)
                dve.wait_ge(rope_read, CT * c + t + 1)
                dve.tensor_tensor(qk[:, t, :], rope_a[t % 2], rope_b[t % 2], ALU.add).then_inc(rope_done, 1)

            def low_x(c):
                for k in range(KD):
                    dve.wait_ge(xT_copied, 2 * KD * c + 2 * k + 2)
                    dve.tensor_tensor(xl[:, k, :], xnT[:, k, :], xh[:, k, :], ALU.subtract).then_inc(xl_ready, 1)

            def chunk(turn, s, last):
                c = turn * CPB + s
                for t in range(CT):
                    rotate(c, s, t)
                    if t >= 1:
                        rotated(c, t - 1)
                rotated(c, CT - 1)
                if not last:
                    dve.wait_ge(xT_ready, KD * (c + 1))
                    normalise(turn, s + 1)
                for j in range(KH):
                    dve.wait_ge(silu_done, KH * c + j + 1)
                    dve.wait_ge(up_done, KH * c + j + 1)
                    dve.wait_ge(hh_done, KH * c + max(j - 2, 0))
                    dve.wait_ge(hl_done, KH * c + max(j - 2, 0))
                    dve.scalar_tensor_tensor(hid[j % 3][:, :], bank_up(j), DEQUANT * H_SCALE, gact[j % 2][:, :],
                                             ALU.mult, ALU.mult).then_inc(hid_done, 1)
                    if isinstance(c, int) and c == 0:
                        moments(BT + 4 * j, 4)
                if isinstance(c, int) and c == 0:
                    inverse(1, BT, BATCH * BT)
                if not last:
                    low_x(c + 1)
                for g in range(4):
                    dve.wait_ge(hi_done, 4 * c + g + 1)
                    dve.wait_ge(mid_done, 4 * c)
                    dve.wait_ge(lo_done, 4 * c)
                    dve.tensor_tensor(rest[g], bank_turn(g), parts[g][:, 0, :], ALU.subtract).then_inc(rest_done, 1)
                for t in range(CT):
                    dve.wait_ge(down_done, CT * c + t // 2 * 2 + 2)
                    if t == 0:
                        dve.wait_ge(biased, CT * (c + 1))
                    row = x_all[:, bass.ds(turn * BT + s * CT + t, 1), :].rearrange("p o d -> p (o d)")
                    dve.scalar_tensor_tensor(row, bank_down(t), DEQUANT / H_SCALE, row, ALU.mult, ALU.add
                                             ).then_inc(y_done, 1)

            dve.tensor_copy(identb[:, :], identf[:, :]).then_inc(weights_ready, 1)
            normalise(0, 0)
            dve.wait_ge(ints_in, 48)
            for w, i in ((wg, int_g), (wu, int_u), (wd, int_d)):
                dve.tensor_copy(w[:, :, :], i).then_inc(weights_ready, 1)
            low_x(0)
            chunk(0, 0, False)
            with dve.Fori(0, BATCH - 1) as i:
                for s in (1, 2):
                    chunk(i, s, False)
            chunk(BATCH - 1, 1, True)

            def maxima(turn, m, h):
                pl, k = m // STEPS, 2 * (m % STEPS) + h
                p = turn * RING + pl
                n = MAXES * p + k
                dve.wait_ge(max_scores, n + 1)
                if k == 0 and not (isinstance(p, int) and p < 2):
                    dve.wait_ge(msplit_done, p - 1)
                dve.tensor_reduce(negmax[pl % 2][:, k:k + 1], ps[:, 2 * (k % 2):2 * (k % 2) + 2, :],
                                  AX.XY, ALU.max, negate=True).then_inc(max_done, 1)

            def rows(p, slot, turn):
                dve.wait_ge(mturned, p + 1)
                if not (isinstance(p, int) and p < 2):
                    dve.wait_ge(m_in[(slot - 2) % RING], 16 * (turn + (slot - 2) // RING + 1))
                n = NPART * MAXES
                dve.tensor_copy(mrows[slot % 2][:, :], ps[0:n, 0, 0:P // 2].bitcast(BF16)).then_inc(mrows_done, 1)

            def invert(p, slot):
                dve.wait_ge(o_stored[slot % 2], 16 * (PER_STEP + 1) * pairs_before(p, slot))
                if not isinstance(p, int) or p >= 2:
                    dve.wait_ge(inv_stored[slot % 2], 16 * (pairs_before(p, slot) - 1))
                dve.reciprocal(invs[slot % 2], sums[slot % 2]).then_inc(inv_done, 1)

            def pairs_before(p, slot):
                return (p - slot % 2) // 2 + 1

            def add_tile(n, k, row):
                dve.wait_ge(wout_done, CREDIT + n + 1)
                dve.wait_ge(res_free[k], 16 * ((n - k) // 2 + 1))
                dve.tensor_tensor(res[k], ps[:, 0, 0:DIM], x_all[:, bass.ds(row, 1), :].rearrange("p o d -> p (o d)"),
                                  ALU.add).then_inc(res_done, 1)

            def step(turn, ls, last_turn=False, tile=None):
                m = ls + LEAD
                q = ls // STEPS
                if ls % STEPS == T_AT and (not last_turn or q + 1 < RING):
                    rows(turn * RING + q + 1, q + 1, turn)
                if tile:
                    add_tile(*tile, tile[0])
                if not last_turn or m < RING * STEPS:
                    maxima(turn, m, 0)
                    maxima(turn, m, 1)
                if ls % STEPS == INV_AT and (q or not isinstance(turn, int)):
                    invert(turn * RING + q - 1, q - 1)

            for m in range(LEAD):
                if m == T_AT + LEAD - STEPS:
                    rows(0, 0, 0)
                maxima(0, m, 0)
                maxima(0, m, 1)
            for ls in range(FIRST):
                step(0, ls)
            with dve.Fori(0, TILES_FROM) as i:
                for ls in range(FIRST, FIRST + RING * STEPS):
                    step(i, ls)
            with dve.Fori(0, TURNS - TILES_FROM) as i:
                for ls in range(FIRST, FIRST + RING * STEPS):
                    j = ls // STEPS - FIRST_SLOT
                    step(i + TILES_FROM, ls, tile=(i * RING + j, j % 2) if ls % STEPS == TILE_AT else None)
            for ls in range(FIRST, RING * STEPS):
                step(TURNS, ls, True, late_tile(ls))

            invert(PAIRS - 1, PAIRS - 1)
            for k in range(CPB):
                dve.wait_ge(last_in[k], 16 * (1 + HG))
                dve.tensor_tensor(olast[k], olast[k], ilast[k], ALU.mult).then_inc(last_divided, 1)
            for t in range(BT):
                dve.wait_ge(wout_done, CREDIT + (BATCH - 1) * BT + t + 1)
                dve.tensor_tensor(rlast[:, t, :], ps[:, t, 0:DIM], x_all[:, (BATCH - 1) * BT + t, :], ALU.add
                                  ).then_inc(last_res, 1)

        @block.gpsimd
        def _(pool):
            pool.memset(mrest[:, 1, :], 0.0).then_inc(divided, CREDIT)
            pool.wait_ge(divided, CREDIT)
            pool.memset(zeros[:, :], 0.0).then_inc(msplit, 1)
            for i in range(2):
                pool.wait_ge(msplit, i + 1)
                pool.memset(mparts[i][:, :], 0.0).then_inc(msplit, 1)
            pool.wait_ge(msplit, 3)
            for i in range(RING):
                pool.memset(ks[i][PROD:ROWS, :, :], 1.0).then_inc(ones_set, 1)
                pool.wait_ge(ones_set, i + 1)

            def chunk(c):
                for j in range(KH):
                    pool.wait_ge(hh_done, KH * c + j + 1)
                    pool.tensor_tensor(hl[:, j, :], hid[j % 3][:, :], hh[:, j, :], ALU.subtract).then_inc(hl_done, 1)
                for g in range(4):
                    pool.wait_ge(mid_done, 4 * c + g + 1)
                    pool.tensor_tensor(parts[g][:, 2, :], rest[g], parts[g][:, 1, :], ALU.subtract
                                       ).then_inc(lo_done, 1)

            with pool.Fori(0, NCHUNK) as c:
                chunk(c)

            def stage_values(p, batch, slot, pair):
                for a in range(2):
                    src = v_all[:, bass.ds(batch * BT, BT), bass.ds(pair * 2 * DH + a * DH, DH)]
                    ins = pool.tensor_copy(vstage[slot % 2][:, a, :, 0:DH], src)
                ins.then_inc(v_staged, 1)

            def split_max(p, slot):
                pool.wait_ge(max_done, MAXES * (p + 1))
                if not (isinstance(p, int) and p < 2):
                    pool.wait_ge(mturned, p - 1)
                nm, mp = negmax[slot % 2][:, :], mparts[slot % 2]
                mc = [mp[:, k * MAXES:(k + 1) * MAXES] for k in range(NPART)]
                n = 4 * p + 3
                pool.tensor_tensor(mc[0], nm, zeros[:, :], ALU.add).then_inc(msplit, 1)
                pool.wait_ge(msplit, n + 1)
                pool.tensor_tensor(mrest[:, 0, :], nm, mc[0], ALU.subtract).then_inc(msplit, 1)
                pool.wait_ge(msplit, n + 2)
                pool.tensor_tensor(mc[1], mrest[:, 0, :], zeros[:, :], ALU.add).then_inc(msplit, 1)
                pool.wait_ge(msplit, n + 3)
                pool.tensor_tensor(mc[2], mrest[:, 0, :], mc[1], ALU.subtract).then_inc(msplit, 1)
                pool.wait_ge(msplit, n + 4)
                pool.tensor_tensor(mrest[:, 1, :], zeros[:, :], zeros[:, :], ALU.add).then_inc(msplit_done, 1)

            pool.wait_ge(y_done, CT * NCHUNK)
            for g in range(4):
                pool.wait_ge(parts_stored[g], 16 * NPART * NCHUNK)
            for i in range(2):
                pool.memset(vstage[i][:, :, :, DH:2 * DH], 1.0).then_inc(ones_set, 1)
                pool.wait_ge(ones_set, RING + i + 1)
            split_max(0, 0)
            pool.wait_ge(v_in, 16 * BATCH)
            stage_values(0, 0, 0, 0)

            def divide(n, k):
                pool.wait_ge(tile_in[k], 16 * (1 + HG) * ((n - k) // 2 + 1))
                pool.wait_ge(wout_done, CREDIT + n - 1)
                pool.tensor_tensor(atile[k], otile[k], itile[k], ALU.mult).then_inc(divided, 1)

            def slot(turn, j, tiles):
                for tile in tiles:
                    divide(*tile)
                q = j + 1
                p = turn * RING + q
                if isinstance(p, int) and p >= PAIRS:
                    return
                split_max(p, q)
                pool.wait_ge(pv_done, STEPS * (p - 1))
                stage_values(p, p // PPB, q, p % PPB)

            for j in range(FIRST_SLOT):
                slot(0, j, [])
            with pool.Fori(0, TILES_FROM) as i:
                for j in range(FIRST_SLOT, FIRST_SLOT + RING):
                    slot(i, j, [])
            with pool.Fori(0, TURNS - TILES_FROM) as i:
                for j in range(RING):
                    slot(i + TILES_FROM, FIRST_SLOT + j, [(i * RING + j, j % 2)])
            for j in range(FIRST_SLOT, RING):
                n = LAST - LAG + 2 * (j - FIRST_SLOT)
                slot(TURNS, j, [(n, n % 2), (n + 1, (n + 1) % 2)])


def rotary_tables():
    inv = np.float32(1.0) / np.power(10000.0, np.arange(0, DH, 2) / DH).astype(np.float32)
    angle = np.outer(np.arange(SEQ, dtype=np.float32), inv).astype(np.float32)
    angle = np.concatenate([angle, angle], axis=-1)
    sign = np.where(np.arange(DH) < DH // 2, -1.0, 1.0).astype(np.float32)
    cos, sin = np.cos(angle), np.sin(angle) * sign
    scale = np.array([DH ** -0.5, 1.0], np.float32)
    both = np.stack([cos, sin], 1)[:, :, None, :] * scale[None, None, :, None]
    both = both.reshape(BT, P, 2, 2, DH).transpose(1, 0, 2, 3, 4)
    return np.ascontiguousarray(both.astype(np.float32))


def kernel(L0_attn_x, L0_attn_Wq, L0_attn_Wkv, L0_attn_Wout, L0_attn_bout,
           L0_ffn_w_gate, L0_ffn_w_up, L0_ffn_w_down):
    import concourse.bacc as bacc
    from concourse.bass_utils import run_bass_kernel_spmd

    laid_out = {
        "x": np.asarray(L0_attn_x),
        "w_q": np.asarray(L0_attn_Wq),
        "w_kv": np.asarray(L0_attn_Wkv),
        "w_out": np.asarray(L0_attn_Wout),
        "b_out": np.asarray(L0_attn_bout),
        "w_gate": np.asarray(L0_ffn_w_gate).T,
        "w_up": np.asarray(L0_ffn_w_up).T,
        "w_down": np.asarray(L0_ffn_w_down).T,
        "rope": rotary_tables(),
        "ident": np.eye(P, dtype=np.float32),
    }
    nc = bacc.Bacc("TRN2", target_bir_lowering=False, num_devices=1)
    arrays, args = {}, []
    for name, a in laid_out.items():
        a = np.ascontiguousarray(a)
        arrays[f"{name}_dram"] = a
        args.append(nc.dram_tensor(f"{name}_dram", a.shape, mybir.dt.from_np(a.dtype), kind="ExternalInput").ap())
    args.append(nc.dram_tensor("out_dram", (BATCH, SEQ, DIM), F32, kind="ExternalOutput").ap())
    build(nc, *args)
    r = run_bass_kernel_spmd(nc, [arrays], core_ids=[0])
    return r.results[0]["out_dram"]
```
